# Optimizing a Trainium2 kernel written in Bass

```python
import numpy as np
import jax
import jax.numpy as jnp

def _softmax(x, axis=-1):
    return jax.nn.softmax(x, axis=axis)

def _gelu(x):
    return jax.nn.gelu(x, approximate=True)

def _silu(x):
    return jax.nn.silu(x)

def _sigmoid(x):
    return jax.nn.sigmoid(x)

def _layernorm(x, axis=-1, eps=1e-05):
    m = jnp.mean(x, axis=axis, keepdims=True)
    v = jnp.var(x, axis=axis, keepdims=True)
    return (x - m) / jnp.sqrt(v + eps)

def _scatter_add(tgt, idx, src, axis=0):
    return tgt.at[idx].add(src)

def _segment_sum(src, seg, n):
    return jax.ops.segment_sum(src, seg, n)
kernel_name = 'mk_dlrm_tower_d1_rec_r8_7936f6'

def setup_inputs(seed: int=0):
    np.random.seed(seed)
    _w = jnp.asarray

    def _rec_inputs():
        import jax
        import jax.numpy as jnp
        _tk = jax.random.key(seed)
        dense_ctx = jax.random.normal(jax.random.fold_in(_tk, 190), (2048, 16), jnp.float32)
        ids = jnp.stack([jax.random.randint(jax.random.fold_in(_tk, 200 + f), (2048,), 0, v, jnp.int32) for f, v in enumerate([12500, 1250, 12500, 1000, 1000, 1250, 1250, 1000, 125000, 12500, 12500, 12500, 1250, 12500, 1000, 1250, 1000, 12500, 12500, 1000, 1250, 1250, 1000, 1000, 1000, 1000, 1000])], axis=1)
        tbl_0 = 0.05 * jax.random.normal(jax.random.fold_in(_tk, 500 + 0), (12500, 128), jnp.float32)
        tbl_1 = 0.05 * jax.random.normal(jax.random.fold_in(_tk, 500 + 1), (1250, 128), jnp.float32)
        tbl_2 = 0.05 * jax.random.normal(jax.random.fold_in(_tk, 500 + 2), (12500, 128), jnp.float32)
        tbl_3 = 0.05 * jax.random.normal(jax.random.fold_in(_tk, 500 + 3), (1000, 128), jnp.float32)
        tbl_4 = 0.05 * jax.random.normal(jax.random.fold_in(_tk, 500 + 4), (1000, 128), jnp.float32)
        tbl_5 = 0.05 * jax.random.normal(jax.random.fold_in(_tk, 500 + 5), (1250, 128), jnp.float32)
        tbl_6 = 0.05 * jax.random.normal(jax.random.fold_in(_tk, 500 + 6), (1250, 128), jnp.float32)
        tbl_7 = 0.05 * jax.random.normal(jax.random.fold_in(_tk, 500 + 7), (1000, 128), jnp.float32)
        tbl_8 = 0.05 * jax.random.normal(jax.random.fold_in(_tk, 500 + 8), (125000, 128), jnp.float32)
        tbl_9 = 0.05 * jax.random.normal(jax.random.fold_in(_tk, 500 + 9), (12500, 128), jnp.float32)
        tbl_10 = 0.05 * jax.random.normal(jax.random.fold_in(_tk, 500 + 10), (12500, 128), jnp.float32)
        tbl_11 = 0.05 * jax.random.normal(jax.random.fold_in(_tk, 500 + 11), (12500, 128), jnp.float32)
        tbl_12 = 0.05 * jax.random.normal(jax.random.fold_in(_tk, 500 + 12), (1250, 128), jnp.float32)
        tbl_13 = 0.05 * jax.random.normal(jax.random.fold_in(_tk, 500 + 13), (12500, 128), jnp.float32)
        tbl_14 = 0.05 * jax.random.normal(jax.random.fold_in(_tk, 500 + 14), (1000, 128), jnp.float32)
        tbl_15 = 0.05 * jax.random.normal(jax.random.fold_in(_tk, 500 + 15), (1250, 128), jnp.float32)
        tbl_16 = 0.05 * jax.random.normal(jax.random.fold_in(_tk, 500 + 16), (1000, 128), jnp.float32)
        tbl_17 = 0.05 * jax.random.normal(jax.random.fold_in(_tk, 500 + 17), (12500, 128), jnp.float32)
        tbl_18 = 0.05 * jax.random.normal(jax.random.fold_in(_tk, 500 + 18), (12500, 128), jnp.float32)
        tbl_19 = 0.05 * jax.random.normal(jax.random.fold_in(_tk, 500 + 19), (1000, 128), jnp.float32)
        tbl_20 = 0.05 * jax.random.normal(jax.random.fold_in(_tk, 500 + 20), (1250, 128), jnp.float32)
        tbl_21 = 0.05 * jax.random.normal(jax.random.fold_in(_tk, 500 + 21), (1250, 128), jnp.float32)
        tbl_22 = 0.05 * jax.random.normal(jax.random.fold_in(_tk, 500 + 22), (1000, 128), jnp.float32)
        tbl_23 = 0.05 * jax.random.normal(jax.random.fold_in(_tk, 500 + 23), (1000, 128), jnp.float32)
        tbl_24 = 0.05 * jax.random.normal(jax.random.fold_in(_tk, 500 + 24), (1000, 128), jnp.float32)
        tbl_25 = 0.05 * jax.random.normal(jax.random.fold_in(_tk, 500 + 25), (1000, 128), jnp.float32)
        tbl_26 = 0.05 * jax.random.normal(jax.random.fold_in(_tk, 500 + 26), (1000, 128), jnp.float32)
        _rk = jax.random.fold_in(_tk, 7)
        W_top1 = 0.0521996 * jax.random.normal(jax.random.fold_in(_tk, 801), (367, 512), jnp.float32)
        W_top2 = 0.0441942 * jax.random.normal(jax.random.fold_in(_tk, 802), (512, 256), jnp.float32)
        W_top3 = 0.0625 * jax.random.normal(jax.random.fold_in(_tk, 803), (256, 1), jnp.float32)
        b_top1 = jnp.zeros((512,), jnp.float32)
        b_top2 = jnp.zeros((256,), jnp.float32)
        return (dense_ctx, ids, tbl_0, tbl_1, tbl_2, tbl_3, tbl_4, tbl_5, tbl_6, tbl_7, tbl_8, tbl_9, tbl_10, tbl_11, tbl_12, tbl_13, tbl_14, tbl_15, tbl_16, tbl_17, tbl_18, tbl_19, tbl_20, tbl_21, tbl_22, tbl_23, tbl_24, tbl_25, tbl_26, W_top1, b_top1, W_top2, b_top2, W_top3)
    dense_ctx, ids, tbl_0, tbl_1, tbl_2, tbl_3, tbl_4, tbl_5, tbl_6, tbl_7, tbl_8, tbl_9, tbl_10, tbl_11, tbl_12, tbl_13, tbl_14, tbl_15, tbl_16, tbl_17, tbl_18, tbl_19, tbl_20, tbl_21, tbl_22, tbl_23, tbl_24, tbl_25, tbl_26, W_top1, b_top1, W_top2, b_top2, W_top3 = _rec_inputs()

    def _L0_rec_setup():
        import jax, jax.numpy as jnp
        import numpy as np
        key = jax.random.key(seed)
        B, F, D = (2048, 27, 128)
        inputs = jax.random.normal(key, (B, F, D), dtype=jnp.float32)
        return {'inputs': inputs, 'num_feas': F}
    _L0_rec_all = _L0_rec_setup()
    _L0_rec_in = {k: v for k, v in _L0_rec_all.items() if k in ()}
    del _L0_rec_all
    return {'dense_ctx': dense_ctx, 'ids': ids, 'tbl_0': tbl_0, 'tbl_1': tbl_1, 'tbl_2': tbl_2, 'tbl_3': tbl_3, 'tbl_4': tbl_4, 'tbl_5': tbl_5, 'tbl_6': tbl_6, 'tbl_7': tbl_7, 'tbl_8': tbl_8, 'tbl_9': tbl_9, 'tbl_10': tbl_10, 'tbl_11': tbl_11, 'tbl_12': tbl_12, 'tbl_13': tbl_13, 'tbl_14': tbl_14, 'tbl_15': tbl_15, 'tbl_16': tbl_16, 'tbl_17': tbl_17, 'tbl_18': tbl_18, 'tbl_19': tbl_19, 'tbl_20': tbl_20, 'tbl_21': tbl_21, 'tbl_22': tbl_22, 'tbl_23': tbl_23, 'tbl_24': tbl_24, 'tbl_25': tbl_25, 'tbl_26': tbl_26, 'W_top1': W_top1, 'b_top1': b_top1, 'W_top2': W_top2, 'b_top2': b_top2, 'W_top3': W_top3}

def reference(dense_ctx, ids, tbl_0, tbl_1, tbl_2, tbl_3, tbl_4, tbl_5, tbl_6, tbl_7, tbl_8, tbl_9, tbl_10, tbl_11, tbl_12, tbl_13, tbl_14, tbl_15, tbl_16, tbl_17, tbl_18, tbl_19, tbl_20, tbl_21, tbl_22, tbl_23, tbl_24, tbl_25, tbl_26, W_top1, b_top1, W_top2, b_top2, W_top3):
    import jax
    import jax.numpy as jnp

    def _L0_rec_ref(inputs, num_feas):
        import jax, jax.numpy as jnp
        import numpy as np
        dot_products = jnp.einsum('bnd,bmd->bnm', inputs, inputs)
        r, c = np.tril_indices(num_feas, k=-1)
        flat_interactions = dot_products[:, c, r]
        return flat_interactions
    e = jnp.stack([tbl_0[ids[:, 0]], tbl_1[ids[:, 1]], tbl_2[ids[:, 2]], tbl_3[ids[:, 3]], tbl_4[ids[:, 4]], tbl_5[ids[:, 5]], tbl_6[ids[:, 6]], tbl_7[ids[:, 7]], tbl_8[ids[:, 8]], tbl_9[ids[:, 9]], tbl_10[ids[:, 10]], tbl_11[ids[:, 11]], tbl_12[ids[:, 12]], tbl_13[ids[:, 13]], tbl_14[ids[:, 14]], tbl_15[ids[:, 15]], tbl_16[ids[:, 16]], tbl_17[ids[:, 17]], tbl_18[ids[:, 18]], tbl_19[ids[:, 19]], tbl_20[ids[:, 20]], tbl_21[ids[:, 21]], tbl_22[ids[:, 22]], tbl_23[ids[:, 23]], tbl_24[ids[:, 24]], tbl_25[ids[:, 25]], tbl_26[ids[:, 26]]], axis=1)
    z = _L0_rec_ref(e, 27)
    z = z.reshape(z.shape[0], -1)
    h = jnp.concatenate([z, dense_ctx], axis=1)
    h = jnp.maximum(h @ W_top1 + b_top1, 0.0)
    h = jnp.maximum(h @ W_top2 + b_top2, 0.0)
    y = h @ W_top3
    return y

_drawn_inputs = setup_inputs


def setup_inputs(seed=0):
    import zlib

    import numpy as np

    out = dict(_drawn_inputs(seed))
    spreads = {'b_top1': (0.0, 0.1), 'b_top2': (0.0, 0.1)}
    factors = {}
    for name, (base, spread) in spreads.items():
        noise = np.random.default_rng([zlib.crc32(name.encode()), seed]).standard_normal(out[name].shape)
        drawn = base * np.exp(spread * noise) if base else spread * noise
        out[name] = jnp.asarray(drawn.astype(out[name].dtype))
    for name, factor in factors.items():
        out[name] = (out[name] * factor).astype(out[name].dtype)
    return out
```

```python
from contextlib import ExitStack

import concourse.bass as bass
from concourse import mybir

F32 = mybir.dt.float32
I32 = mybir.dt.int32
ALU = mybir.AluOpType
ACT = mybir.ActivationFunctionType

P = 128
TILES = 4
STRIP = 32
STRIPS = P // STRIP
BANK = 512


def dlrm_tower(nc, dense_ctx, ids, tables, W_top1, b_top1, W_top2, b_top2, W_top3, y):
    B, NF = ids.shape
    ND = dense_ctx.shape[1]
    D = tables[0].shape[1]
    K1, N1 = W_top1.shape
    N2 = W_top2.shape[1]
    PAIRS = NF * (NF - 1) // 2
    assert D == P and K1 == PAIRS + ND and N1 % P == 0 and N2 % P == 0 and NF <= STRIP

    BLOCK = TILES * P
    BLOCKS = B // BLOCK
    assert B % BLOCK == 0 and BLOCK == BANK
    M1, M2 = N1 // P, N2 // P
    KC = -(-K1 // P)
    KROWS = [min(P, K1 - c * P) for c in range(KC)]

    T_FEATS = [list(range(f, min(f + 4, NF))) for f in range(0, NF, 4)]
    T_FILLS = len(T_FEATS)
    T_PER_BANK = TILES * T_FILLS // 2
    assert TILES * T_FILLS % 2 == 0
    GROUPS = P // STRIPS
    HALF = GROUPS // 2
    assert HALF * NF <= BANK
    Z_COLS = [list(range(n, min(n + 4, NF))) for n in range(1, NF, 4)]
    WORK = ([("Z", i) for i in range(len(Z_COLS))] + [("H", c) for c in range(KC)]
            + [("L1", m) for m in range(M1)] + [("L2", m) for m in range(M2)] + [("Y", 0)])
    NW = len(WORK)
    WORK_AT = {w: i for i, w in enumerate(WORK)}
    WB = 4

    def uses_before(i):
        return i // WB

    def uses_per_block(bank):
        return len(range(bank, NW, WB))

    ids_v = ids.rearrange("(t p) f -> p t f", p=P)
    dense_v = dense_ctx.rearrange("(k s g) c -> s k g c", s=P, g=STRIPS)
    y_v = y.rearrange("(k n) o -> o k n", k=BLOCKS)

    with ExitStack() as ctx:
        def sb(name, shape, dt=F32):
            return ctx.enter_context(nc.sbuf_tensor(name, shape, dt))

        def psum(name, shape):
            return ctx.enter_context(nc.psum_tensor(name, shape, F32))

        def sem(name):
            return ctx.enter_context(nc.semaphore(name))

        idx = sb("idx", [P, TILES, NF], I32)
        rows = sb("rows", [P, TILES, NF, D])
        et = sb("et", [P, 2, P, STRIP])
        z = sb("z", [P, P, NF])
        h = sb("h", [P, STRIPS, K1])
        hT = sb("hT", [P, KC, BLOCK])
        a1T = sb("a1T", [P, M1, BLOCK])
        a2T = sb("a2T", [P, M2, BLOCK])
        y_row = sb("y_row", [1, BLOCK])
        w1 = sb("w1", [P, KC, N1])
        w2 = sb("w2", [P, M1, N2])
        NV = M1 + 2 * M2
        vec_rows = sb("vec_rows", [NV, P])
        vec_cols = sb("vec_cols", [P, NV])
        b1, b2, w3 = vec_cols[:, 0:M1], vec_cols[:, M1:M1 + M2], vec_cols[:, M1 + M2:NV]
        ident = sb("ident", [P, P])

        t_bank = [psum(f"t_bank{i}", [P, BANK]) for i in range(2)]
        g_bank = [psum(f"g_bank{i}", [P, BANK]) for i in range(2)]
        w_bank = [psum(f"w_bank{i}", [P, BANK]) for i in range(WB)]

        weights_in = sem("weights_in")
        vectors_in = sem("vectors_in")
        vectors_transposed = sem("vectors_transposed")
        vectors_ready = sem("vectors_ready")
        ident_zeroed = sem("ident_zeroed")
        ident_ready = sem("ident_ready")
        et_padded = sem("et_padded")
        idx_ready = [sem(f"idx_ready{j}") for j in range(TILES)]
        tile_started = sem("tile_started")
        rows_ready = [sem(f"rows_ready{j}") for j in range(TILES)]
        t_filled = sem("t_filled")
        t_drained = [sem(f"t_drained{i}") for i in range(2)]
        g_filled = sem("g_filled")
        g_drained = [sem(f"g_drained{i}") for i in range(2)]
        w_filled = sem("w_filled")
        w_drained = [sem(f"w_drained{i}") for i in range(WB)]
        dense_in = sem("dense_in")
        y_row_ready = sem("y_row_ready")
        y_row_free = sem("y_row_free")
        y_out = sem("y_out")

        WEIGHT_DMAS = KC + 1
        block = ctx.enter_context(nc.Block())

        @block.sync
        def _(sp):
            for j in range(TILES):
                sp.dma_start(idx[:, j, :], ids_v[:, j, :]).then_inc(idx_ready[j], 16)
            sp.dma_start(vec_rows[0:M1, :], b_top1.rearrange("(m p) -> m p", p=P)).then_inc(vectors_in, 16)
            sp.dma_start(vec_rows[M1:M1 + M2, :], b_top2.rearrange("(m p) -> m p", p=P)).then_inc(vectors_in, 16)
            sp.dma_start(vec_rows[M1 + M2:NV, :], W_top3.rearrange("(m p) o -> m (p o)", p=P)
                         ).then_inc(vectors_in, 16)
            for c in range(KC):
                sp.dma_start(w1[0:KROWS[c], c, :], W_top1[c * P:c * P + KROWS[c], :]).then_inc(weights_in, 16)
            sp.dma_start(w2[:], W_top2.rearrange("(k p) n -> p k n", p=P)).then_inc(weights_in, 16)
            sp.dma_start(h[:, :, PAIRS:K1], dense_v[:, 0, :, :]).then_inc(dense_in, 16)
            sp.sem_inc(y_row_free, 1)

            def store_y(k):
                sp.wait_ge(y_row_ready, k + 1)
                sp.dma_start(y_v[:, bass.ds(k, 1), :], y_row[:, :]).then_inc(y_out, 16)
                sp.wait_ge(y_out, 16 * (k + 1))
                sp.sem_inc(y_row_free, 1)

            with sp.Fori(1, BLOCKS) as k:
                for j in range(TILES):
                    sp.wait_ge(rows_ready[j], 16 * NF * k)
                    sp.dma_start(idx[:, j, :], ids_v[:, bass.ds(TILES * k + j, 1), :]).then_inc(idx_ready[j], 16)
                sp.wait_ge(w_filled, NW * (k - 1) + WORK_AT["H", KC - 1] + 1)
                sp.dma_start(h[:, :, PAIRS:K1], dense_v[:, bass.ds(k, 1), :, :]).then_inc(dense_in, 16)
                store_y(k - 1)
            store_y(BLOCKS - 1)

        @block.gpsimd
        def _(pool):
            nc.gpsimd.memset(ident[:], 0.0).then_inc(ident_zeroed, 1)
            pool.wait_ge(ident_zeroed, 1)
            nc.gpsimd.affine_select(out=ident[:], in_=ident[:], compare_op=ALU.not_equal, fill=1.0, base=0,
                                    pattern=[[-1, P]], channel_multiplier=1).then_inc(ident_ready, 1)
            with pool.Fori(0, BLOCKS) as k:
                for j in range(TILES):
                    done = (j + 1) * T_FILLS
                    pool.wait_ge(t_drained[0], T_PER_BANK * k + (done + 1) // 2)
                    pool.wait_ge(t_drained[1], T_PER_BANK * k + done // 2)
                    pool.wait_ge(idx_ready[j], 16 * (k + 1))
                    pool.sem_inc(tile_started, 1)
                    for f in range(NF):
                        pool.indirect_dma_start(
                            rows[:, j, f, :], None, tables[f],
                            bass.IndirectOffsetOnAxis(ap=idx[:, j, f:f + 1], axis=0)).then_inc(rows_ready[j], 16)

        @block.tensor
        def _(pe):
            pe.wait_ge(ident_ready, 1)
            pe.wait_ge(vectors_in, 48)
            nc.tensor.transpose(w_bank[0][:, 0:NV], vec_rows[:], ident[0:NV, 0:NV]).then_inc(vectors_transposed, 1)

            def transpose_tile(k, j):
                pe.wait_ge(rows_ready[j], 16 * NF * (k + 1))
                for i, feats in enumerate(T_FEATS):
                    n = j * T_FILLS + i
                    pe.wait_ge(t_drained[n % 2], T_PER_BANK * (k + 1) + n // 2)
                    for q, f in enumerate(feats):
                        last = nc.tensor.transpose(t_bank[n % 2][:, q * P:(q + 1) * P], rows[:, j, f, :], ident[:])
                    last.then_inc(t_filled, 1)

            def gram_tile(k, j):
                done = (j + 1) * T_FILLS
                pe.wait_ge(t_drained[0], T_PER_BANK * (k + 1) + (done + 1) // 2)
                pe.wait_ge(t_drained[1], T_PER_BANK * (k + 1) + done // 2)
                for half in range(2):
                    pe.wait_ge(g_drained[half], TILES * k + j + 1)
                    for s in range(HALF):
                        for g in range(STRIPS):
                            b = (half * HALF + s) * STRIPS + g
                            last = nc.tensor.matmul(
                                g_bank[half][g * STRIP:(g + 1) * STRIP, s * NF:(s + 1) * NF],
                                et[:, j % 2, b, :], et[:, j % 2, b, 0:NF], start=True, stop=True)
                    last.then_inc(g_filled, 1)

            def bank_for(k, w):
                i = WORK_AT[w]
                pe.wait_ge(w_drained[i % WB], uses_per_block(i % WB) * k + uses_before(i) + 1)
                return w_bank[i % WB]

            def drained(k, w):
                i = WORK_AT[w]
                pe.wait_ge(w_drained[i % WB], uses_per_block(i % WB) * k + uses_before(i) + 2)

            with pe.Fori(0, BLOCKS) as k:
                transpose_tile(k, 0)
                pe.wait_ge(et_padded, 1)
                for j in range(1, TILES):
                    transpose_tile(k, j)
                    gram_tile(k, j - 1)
                gram_tile(k, TILES - 1)

                for half in range(2):
                    pe.wait_ge(g_drained[half], TILES * (k + 1) + 1)
                for i, cols in enumerate(Z_COLS):
                    bank = bank_for(k, ("Z", i))
                    for q, n in enumerate(cols):
                        last = nc.tensor.transpose(bank[:, q * P:(q + 1) * P], z[:, :, n], ident[:])
                    last.then_inc(w_filled, 1)

                for i in range(len(Z_COLS)):
                    drained(k, ("Z", i))
                pe.wait_ge(dense_in, 16 * (k + 1))
                for c in range(KC):
                    bank = bank_for(k, ("H", c))
                    for g in range(STRIPS):
                        last = nc.tensor.transpose(bank[0:KROWS[c], g * P:(g + 1) * P],
                                                   h[:, g, c * P:c * P + KROWS[c]], ident[:])
                    last.then_inc(w_filled, 1)

                pe.wait_ge(weights_in, 16 * WEIGHT_DMAS)
                for c in range(KC):
                    drained(k, ("H", c))
                for m in range(M1):
                    bank = bank_for(k, ("L1", m))
                    for c in range(KC):
                        last = nc.tensor.matmul(bank[:], w1[0:KROWS[c], c, m * P:(m + 1) * P], hT[0:KROWS[c], c, :],
                                                start=(c == 0), stop=(c == KC - 1))
                    last.then_inc(w_filled, 1)
                for m in range(M1):
                    drained(k, ("L1", m))
                for m in range(M2):
                    bank = bank_for(k, ("L2", m))
                    for c in range(M1):
                        last = nc.tensor.matmul(bank[:], w2[:, c, m * P:(m + 1) * P], a1T[:, c, :],
                                                start=(c == 0), stop=(c == M1 - 1))
                    last.then_inc(w_filled, 1)
                for m in range(M2):
                    drained(k, ("L2", m))
                bank = bank_for(k, ("Y", 0))
                for c in range(M2):
                    last = nc.tensor.matmul(bank[0:1, :], w3[:, c:c + 1], a2T[:, c, :],
                                            start=(c == 0), stop=(c == M2 - 1))
                last.then_inc(w_filled, 1)

        def t_out(j, i):
            feats = T_FEATS[i]
            n = j * T_FILLS + i
            return (et[:, j % 2, :, feats[0]:feats[-1] + 1],
                    t_bank[n % 2][:, 0:len(feats) * P].rearrange("p (f b) -> p b f", b=P))

        def z_out(j, half):
            s0 = j * GROUPS + half * HALF
            return (z[:, s0:s0 + HALF, :], g_bank[half][:, 0:HALF * NF].rearrange("p (s n) -> p s n", n=NF))

        T_G_ORDER = [("T", 0)]
        for j in range(1, TILES):
            T_G_ORDER += [("T", j), ("G", j - 1)]
        T_G_ORDER += [("G", TILES - 1)]

        @block.scalar
        def _(act):
            act.sem_inc(t_drained[0], T_PER_BANK)
            act.sem_inc(g_drained[0], 1)

            with act.Fori(0, BLOCKS) as k:
                for what, j in T_G_ORDER:
                    if what == "T":
                        for i in range(T_FILLS):
                            n = j * T_FILLS + i
                            if n % 2 == 0:
                                act.wait_ge(t_filled, TILES * T_FILLS * k + n + 1)
                                out, src = t_out(j, i)
                                nc.scalar.activation(out, src, ACT.Copy).then_inc(t_drained[0], 1)
                    else:
                        act.wait_ge(g_filled, 2 * TILES * k + 2 * j + 1)
                        out, src = z_out(j, 0)
                        nc.scalar.activation(out, src, ACT.Copy).then_inc(g_drained[0], 1)
                for c in range(KC):
                    i = WORK_AT["H", c]
                    act.wait_ge(w_filled, NW * k + i + 1)
                    nc.scalar.activation(hT[0:KROWS[c], c, :], w_bank[i % WB][0:KROWS[c], :],
                                         ACT.Copy).then_inc(w_drained[i % WB], 1)
                act.wait_ge(vectors_ready, 1)
                for name, bias, dst, chunks in (("L1", b1, a1T, M1), ("L2", b2, a2T, M2)):
                    for m in range(0, chunks, 2):
                        i = WORK_AT[name, m]
                        act.wait_ge(w_filled, NW * k + i + 1)
                        nc.scalar.activation(dst[:, m, :], w_bank[i % WB][:], ACT.Relu,
                                             bias=bias[:, m:m + 1]).then_inc(w_drained[i % WB], 1)

        @block.vector
        def _(dve):
            dve.sem_inc(t_drained[1], T_PER_BANK)
            dve.sem_inc(g_drained[1], 1)
            dve.wait_ge(vectors_transposed, 1)
            nc.vector.tensor_copy(vec_cols[:], w_bank[0][:, 0:NV]).then_inc(vectors_ready, 1)
            dve.wait_ge(vectors_ready, 1)
            for i in range(WB):
                dve.sem_inc(w_drained[i], 1)
            nc.vector.memset(et[:, :, :, NF:STRIP], 0.0).then_inc(et_padded, 1)

            with dve.Fori(0, BLOCKS) as k:
                for what, j in T_G_ORDER:
                    if what == "T":
                        for i in range(T_FILLS):
                            n = j * T_FILLS + i
                            if n % 2 == 1:
                                dve.wait_ge(t_filled, TILES * T_FILLS * k + n + 1)
                                out, src = t_out(j, i)
                                nc.vector.tensor_copy(out, src).then_inc(t_drained[1], 1)
                    else:
                        dve.wait_ge(g_filled, 2 * TILES * k + 2 * j + 2)
                        out, src = z_out(j, 1)
                        nc.vector.tensor_copy(out, src).then_inc(g_drained[1], 1)
                for i, cols in enumerate(Z_COLS):
                    w = WORK_AT["Z", i]
                    dve.wait_ge(w_filled, NW * k + w + 1)
                    for q, n in enumerate(cols):
                        first = n * (n - 1) // 2
                        src = w_bank[w % WB][:, q * P:(q + 1) * P].rearrange("p (g m) -> p g m", m=STRIP)
                        last = nc.vector.tensor_copy(h[:, :, first:first + n], src[:, :, 0:n])
                    last.then_inc(w_drained[w % WB], 1)
                for name, bias, dst, chunks in (("L1", b1, a1T, M1), ("L2", b2, a2T, M2)):
                    for m in range(1, chunks, 2):
                        i = WORK_AT[name, m]
                        dve.wait_ge(w_filled, NW * k + i + 1)
                        nc.vector.tensor_scalar(dst[:, m, :], w_bank[i % WB][:], bias[:, m:m + 1], 0.0,
                                                ALU.add, ALU.max).then_inc(w_drained[i % WB], 1)
                i = WORK_AT["Y", 0]
                dve.wait_ge(w_filled, NW * k + i + 1)
                dve.wait_ge(y_row_free, k + 1)
                nc.vector.tensor_copy(y_row[:, :].rearrange("p (s g) -> p g s", g=STRIPS),
                                      w_bank[i % WB][0:1, :].rearrange("p (g s) -> p g s", g=STRIPS)
                                      ).then_inc(y_row_ready, 1)
                dve.wait_ge(y_row_ready, k + 1)
                dve.sem_inc(w_drained[i % WB], 1)


NAMES = (["dense_ctx", "ids"] + [f"tbl_{f}" for f in range(27)]
         + ["W_top1", "b_top1", "W_top2", "b_top2", "W_top3"])


def kernel(**inputs):
    import numpy as np
    import concourse.bacc as bacc
    from concourse.bass_utils import run_bass_kernel_spmd

    nc = bacc.Bacc("TRN2", target_bir_lowering=False, num_devices=1)
    arrays, aps = {}, {}
    for name in NAMES:
        a = np.ascontiguousarray(inputs[name])
        arrays["in_" + name] = a
        aps[name] = nc.dram_tensor("in_" + name, a.shape, mybir.dt.from_np(a.dtype), kind="ExternalInput").ap()
    out = nc.dram_tensor("out_y", (inputs["ids"].shape[0], 1), F32, kind="ExternalOutput").ap()
    tables = [aps[n] for n in NAMES if n.startswith("tbl_")]
    dlrm_tower(nc, aps["dense_ctx"], aps["ids"], tables, aps["W_top1"], aps["b_top1"], aps["W_top2"],
               aps["b_top2"], aps["W_top3"], out)
    result = run_bass_kernel_spmd(nc, [arrays], core_ids=[0])
    return result.results[0]["out_y"]
```

```python
from contextlib import ExitStack

import concourse.bass as bass
from concourse import mybir

F32 = mybir.dt.float32
F32R = mybir.dt.float32r
F16 = mybir.dt.float16
I32 = mybir.dt.int32
ALU = mybir.AluOpType
ACT = mybir.ActivationFunctionType

P = 128
UNIT_TILES = 2
UNIT = UNIT_TILES * P
SLOTS = 2
STRIP = 32
QUADS = P // STRIP
BANK = 512
ONE_HOT = (14, 16, 19, 22, 23, 24, 25, 26)
PIECE = 4


def dlrm_tower(nc, dense_ctx, ids, tables, W_top1, b_top1, W_top2, b_top2, W_top3, y):
    B, NF = ids.shape
    ND = dense_ctx.shape[1]
    D = tables[0].shape[1]
    K1, N1 = W_top1.shape
    N2 = W_top2.shape[1]
    PAIRS = NF * (NF - 1) // 2
    UNITS = B // UNIT
    assert PAIRS > (K1 - 1) // P * P
    assert D == P and K1 == PAIRS + ND and N1 % P == 0 and N2 % P == 0 and NF <= STRIP
    assert B % (SLOTS * UNIT) == 0

    OC = 8
    V = tables[ONE_HOT[0]].shape[0]
    OP = V // OC
    assert all(tables[f].shape[0] == V for f in ONE_HOT) and OP * OC == V and OP <= P and OC % PIECE == 0
    assert OP % 16
    assert V <= 2048
    NOH = len(ONE_HOT)
    PIECES = OC // PIECE

    GATHERED = [f for f in range(NF) if f not in ONE_HOT]
    NG = len(GATHERED)
    T_FEATS = []
    for f in GATHERED:
        if T_FEATS and T_FEATS[-1][-1] == f - 1 and len(T_FEATS[-1]) < 4:
            T_FEATS[-1].append(f)
        else:
            T_FEATS.append([f])
    NT = len(T_FEATS)

    GROUPS = UNIT // QUADS
    G_CHUNKS = NOH
    G_TILE = G_CHUNKS // UNIT_TILES
    G_HALF = GROUPS // G_CHUNKS // 2
    GW = QUADS * NF
    GROWS = (QUADS - 1) * STRIP + NF
    assert G_HALF * 2 * G_CHUNKS == GROUPS and G_HALF * GW <= BANK

    M1, M2 = N1 // P, N2 // P
    KC = -(-K1 // P)
    KROWS = [min(P, K1 - c * P) for c in range(KC)]
    WORK = ([("H", c) for c in range(KC)] + [("L1", m) for m in range(M1)]
            + [("L2", m) for m in range(M2)] + [("Y", 0)])
    NW = len(WORK)
    WORK_AT = {w: i for i, w in enumerate(WORK)}
    WB = 3
    W_USES = [len(range(bank, NW, WB)) for bank in range(WB)]

    ids_v = ids.rearrange("(t p) f -> p t f", p=P)
    dense_v = dense_ctx.rearrange("(u j p) c -> p u j c", j=UNIT_TILES, p=P)
    y_v = y.rearrange("(u n) o -> o u n", u=UNITS)

    with ExitStack() as ctx:
        def sb(name, shape, dt=F32):
            return ctx.enter_context(nc.sbuf_tensor(name, shape, dt))

        def psum(name, shape):
            return ctx.enter_context(nc.psum_tensor(name, shape, F32))

        def sem(name):
            return ctx.enter_context(nc.semaphore(name))

        TILES = SLOTS * UNIT_TILES
        idx = sb("idx", [P, TILES, NF], I32)
        rows = sb("rows", [P, TILES, NG, D])
        et = sb("et", [P, SLOTS, UNIT, STRIP])
        z = sb("z", [P, GROUPS, NF])
        zt = sb("zt", [P, UNIT_TILES, NF - 1, STRIP])
        h = sb("h", [P, UNIT_TILES, K1])
        hT = z[:].rearrange("p s n -> p (s n)")[:, 0:KC * UNIT].rearrange("p (c b) -> p c b", c=KC)
        a1T = zt[:].rearrange("p j n m -> p (j n m)")[:, 0:M1 * UNIT].rearrange("p (m b) -> p m b", m=M1)
        a2T = hT[:, 0:M2, :]
        y_row = sb("y_row", [1, UNIT])
        w1 = sb("w1", [P, KC, N1])
        w2 = sb("w2", [P, M1, N2])
        NV = M1 + 2 * M2
        vec_rows = sb("vec_rows", [NV, P])
        vec_cols = sb("vec_cols", [P, NV])
        b1, b2, w3 = vec_cols[:, 0:M1], vec_cols[:, M1:M1 + M2], vec_cols[:, M1 + M2:NV]
        ident = sb("ident", [P, P])
        ident_h = sb("ident_h", [NOH, NOH], F16)
        row_no_i = sb("row_no_i", [OP, OC], I32)
        row_no = sb("row_no", [OP, OC])
        table_hi = sb("table_hi", [OP, NOH, OC, D], F32R)
        table_lo = sb("table_lo", [OP, NOH, OC, D], F32R)
        one_hot = sb("one_hot", [OP, PIECES, PIECE, UNIT], F32R)
        idsT = sb("idsT", [NOH, B], F16)
        stage = [rows[0:OP, TILES - 1, OC * i:OC * (i + 1), :] for i in range(2)]
        ids_i = rows[:, TILES - 2, 0:4, :].rearrange("p a d -> p (a d)").bitcast(I32)[:, 0:B // P * NF] \
            .rearrange("p (t f) -> p t f", f=NF)
        ids_f = zt[:].rearrange("p j n m -> p (j n m)")[:, 0:B // P * NOH].rearrange("p (t f) -> p t f", f=NOH)

        e_bank = [psum(f"e_bank{i}", [P, BANK]) for i in range(2)]
        id_bank = psum("id_bank", [P, UNIT])
        g_banks = psum("g_banks", [P, 2, BANK])
        w_bank = [psum(f"w_bank{i}", [P, BANK]) for i in range(WB)]

        weights_in = sem("weights_in")
        vectors_in = sem("vectors_in")
        vectors_transposed = sem("vectors_transposed")
        vectors_ready = sem("vectors_ready")
        ident_zeroed = sem("ident_zeroed")
        ident_ready = sem("ident_ready")
        row_no_made = sem("row_no_made")
        pads_ready = sem("pads_ready")
        ids_in = sem("ids_in")
        ids_float = sem("ids_float")
        ids_transposed = sem("ids_transposed")
        idsT_ready = sem("idsT_ready")
        table_in = [sem(f"table_in{i}") for i in range(2)]
        hi_ready = sem("hi_ready")
        lo_ready = sem("lo_ready")
        idx_ready = [sem(f"idx_ready{j}") for j in range(TILES)]
        tile_started = sem("tile_started")
        rows_ready = [sem(f"rows_ready{j}") for j in range(TILES)]
        broadcast_begun = sem("broadcast_begun")
        ids_broadcast = sem("ids_broadcast")
        one_hot_ready = sem("one_hot_ready")
        one_hot_used = sem("one_hot_used")
        t_filled = sem("t_filled")
        e_drained = [sem(f"e_drained{i}") for i in range(2)]
        g_filled = sem("g_filled")
        g_drained = [sem(f"g_drained{q}") for q in range(QUADS)]
        z_turned = sem("z_turned")
        pairs_packed = sem("pairs_packed")
        w_filled = sem("w_filled")
        w_drained = [sem(f"w_drained{i}") for i in range(WB)]
        dense_in = sem("dense_in")
        y_row_ready = sem("y_row_ready")
        y_row_free = sem("y_row_free")
        y_out = sem("y_out")

        WEIGHT_DMAS = KC + 1
        SPLIT_LEAD = 2
        ROWS_OF_TILE = 16 * NG

        def steps(has_next):
            def oh(*qs):
                return [("OH", q) for q in qs] if has_next else []

            def t0(a, b):
                return [("T0", i) for i in range(a, b)] if has_next else []

            def work(kind):
                return [("W", n) for n, w in enumerate(WORK) if w[0] == kind]

            out = []
            for q in range(G_TILE):
                out += [("G", q)] + oh(q) + [("T1", i) for i in range(2 * q, min(2 * q + 2, NT))]
            for q in range(G_TILE, G_CHUNKS - 1):
                out += [("G", q)] + oh(q) + t0(q - G_TILE, q - G_TILE + 1)
            out += [("G", G_CHUNKS - 1), ("ZT", 0)] + t0(G_TILE - 1, G_TILE) + oh(NOH - 1) + t0(G_TILE, NT - 2)
            return out + work("H") + t0(NT - 2, NT - 1) + work("L1") + work("L2") + t0(NT - 1, NT) + work("Y")

        MAKE_AFTER = {("OH", q - 1): q for q in range(1, NOH)}

        E_STEPS = [s for s in steps(True) if s[0] in ("OH", "T0", "T1")]
        FIRST_STEPS = [s for s in E_STEPS if s[0] != "T1"]
        E_AT = {s: n for n, s in enumerate(E_STEPS)}
        FIRST, LAST = -1, UNITS - 1
        E_LEAD = len(E_STEPS)
        assert len(E_STEPS) % 2 == 0
        E_PER_BANK = len(E_STEPS) // 2

        def e_missing(bank):
            return len([n for s, n in E_AT.items() if s[0] == "T1" and n % 2 == bank])

        def e_drains_before(rnd, n, bank):
            earlier = [s for s, m in E_AT.items() if m < n and m % 2 == bank]
            if rnd is FIRST:
                earlier = [s for s in earlier if s[0] != "T1"] + [None] * e_missing(bank)
            if rnd is LAST:
                earlier = [s for s in earlier if s[0] == "T1"]
            return E_LEAD + E_PER_BANK * (rnd + 1) + len(earlier)

        def t_fills_until(rnd, kind, i):
            return 2 * NT * (rnd + 1) + (NT if kind == "T0" else 0) + i + 1

        G_ENGINE = ["act", "act", "act", "dve"]

        def w_engine(kind, i):
            return "act" if kind == "Y" or i % 2 == 0 else "dve"

        def e_engine(kind, i):
            return "dve" if kind == "T0" and G_TILE - 1 <= i < NT - 2 else "act"

        def copy(eng, out, src):
            if eng == "act":
                return nc.scalar.activation(out, src, ACT.Copy)
            return nc.vector.tensor_copy(out, src)

        def drain_e(me, engine, rnd, slot, kind, i):
            if e_engine(kind, i) != me:
                return
            n = E_AT[kind, i]
            bank = e_bank[n % 2]
            if kind == "OH":
                engine.wait_ge(one_hot_used, PIECES * (NOH * (rnd + 1) + i + 1) + PIECES)
                out = et[:, (slot + 1) % SLOTS, :, ONE_HOT[i]].rearrange("p (j s g) -> p j s g", g=QUADS, s=STRIP)
                src = bank[:, 0:UNIT].rearrange("p (j g s) -> p j s g", g=QUADS, s=STRIP)
            else:
                engine.wait_ge(t_filled, t_fills_until(rnd, kind, i))
                feats = T_FEATS[i]
                to, j = (slot, 1) if kind == "T1" else ((slot + 1) % SLOTS, 0)
                out = et[:, to, j * P:(j + 1) * P, feats[0]:feats[-1] + 1].rearrange("p (s g) f -> p s g f", g=QUADS)
                src = bank[:, 0:len(feats) * P].rearrange("p (f g s) -> p s g f", g=QUADS, s=STRIP)
            copy(me, out, src).then_inc(e_drained[n % 2], 1)

        def drain_g(me, engine, u, q):
            waited = False
            for g in range(QUADS):
                if G_ENGINE[g] != me:
                    continue
                if not waited:
                    engine.wait_ge(g_filled, G_CHUNKS * u + q + 1)
                    waited = True
                strip = slice(g * STRIP, g * STRIP + NF)
                src = g_banks[strip, :, 0:G_HALF * GW].rearrange("p k (s c) -> p k s c", c=GW)
                out = z[strip, 2 * G_HALF * q:2 * G_HALF * (q + 1), :].rearrange("p (k s) n -> p k s n", k=2)
                copy(me, out, src[:, :, :, g * NF:(g + 1) * NF]).then_inc(g_drained[g], 1)

        def drain_w(me, engine, u, n):
            kind, i = WORK[n]
            if w_engine(kind, i) != me:
                return
            engine.wait_ge(w_filled, NW * u + n + 1)
            bank, done = w_bank[n % WB], w_drained[n % WB]
            if kind == "H":
                copy(me, hT[0:KROWS[i], i, :], bank[0:KROWS[i], 0:UNIT]).then_inc(done, 1)
            elif kind in ("L1", "L2"):
                bias, out = (b1, a1T) if kind == "L1" else (b2, a2T)
                if me == "act":
                    nc.scalar.activation(out[:, i, :], bank[:, 0:UNIT], ACT.Relu, bias=bias[:, i:i + 1]
                                         ).then_inc(done, 1)
                else:
                    nc.vector.tensor_scalar(out[:, i, :], bank[:, 0:UNIT], bias[:, i:i + 1], 0.0,
                                            ALU.add, ALU.max).then_inc(done, 1)
            else:
                engine.wait_ge(y_row_free, u + 1)
                copy(me, y_row[:, :], bank[0:1, 0:UNIT]).then_inc(y_row_ready, 1)
                engine.wait_ge(y_row_ready, u + 1)
                engine.sem_inc(done, 1)

        def turn_tile(dve, u, j):
            for g in range(QUADS):
                dve.wait_ge(g_drained[g], G_CHUNKS * u + (j + 1) * G_TILE + 1)
            nc.vector.transpose(zt[:, j, :, :], z[:, j * STRIP:(j + 1) * STRIP, 1:NF].rearrange("p s n -> p n s")
                                ).then_inc(z_turned, 1)

        def pack_pairs(act, u):
            act.wait_ge(z_turned, UNIT_TILES * (u + 1))
            chunk = 0
            for n in range(1, NF):
                first = n * (n - 1) // 2
                last = nc.scalar.activation(h[:, :, first:first + n], zt[:, :, n - 1, 0:n], ACT.Copy)
                if first + n >= min((chunk + 1) * P, PAIRS):
                    last.then_inc(pairs_packed, 1)
                    chunk += 1
            assert chunk == KC

        def drain_steps(me, engine, u, slot, has_next):
            if me == "dve" and has_next:
                make_one_hot(engine, u + 1, 0)
            for kind, i in steps(has_next):
                if kind == "G":
                    drain_g(me, engine, u, i)
                elif kind == "ZT":
                    if me == "dve":
                        turn_tile(engine, u, 1)
                    else:
                        pack_pairs(engine, u)
                elif kind == "W":
                    drain_w(me, engine, u, i)
                else:
                    drain_e(me, engine, u, slot, kind, i)
                    if me == "dve" and (kind, i) == ("T1", NT - 1):
                        turn_tile(engine, u, 0)
                if me == "dve" and (kind, i) in MAKE_AFTER and has_next:
                    make_one_hot(engine, u + 1, MAKE_AFTER[kind, i])

        def make_one_hot(dve, u, q):
            for piece in range(PIECES):
                if piece == 0:
                    dve.wait_ge(ids_broadcast, NOH * u + q + 1)
                dve.wait_ge(one_hot_used, PIECES * (NOH * u + q) + piece + 1)
                nc.vector.tensor_tensor(
                    one_hot[:, piece, :, :],
                    id_bank[0:OP, :].unsqueeze(1).broadcast_to([OP, PIECE, UNIT]),
                    row_no[:, piece * PIECE:(piece + 1) * PIECE].unsqueeze(2).broadcast_to([OP, PIECE, UNIT]),
                    ALU.is_equal).then_inc(one_hot_ready, 1)

        block = ctx.enter_context(nc.Block())

        @block.sync
        def _(sp):
            for j in range(TILES):
                sp.dma_start(idx[:, j, :], ids_v[:, j, :]).then_inc(idx_ready[j], 16)
            sp.dma_start(ids_i, ids_v).then_inc(ids_in, 16)
            sp.dma_start(vec_rows[0:M1, :], b_top1.rearrange("(m p) -> m p", p=P)).then_inc(vectors_in, 16)
            sp.dma_start(vec_rows[M1:M1 + M2, :], b_top2.rearrange("(m p) -> m p", p=P)).then_inc(vectors_in, 16)
            sp.dma_start(vec_rows[M1 + M2:NV, :], W_top3.rearrange("(m p) o -> m (p o)", p=P)
                         ).then_inc(vectors_in, 16)
            for q, f in enumerate(ONE_HOT):
                if q >= 2:
                    sp.wait_ge(lo_ready, q - 1)
                table = tables[f].rearrange("(p c) d -> p c d", c=OC)
                for part in (slice(0, OP // 16 * 16), slice(OP // 16 * 16, OP)):
                    sp.dma_start(stage[q % 2][part], table[part]).then_inc(table_in[q % 2], 16)
            for c in range(KC):
                sp.dma_start(w1[0:KROWS[c], c, :], W_top1[c * P:c * P + KROWS[c], :]).then_inc(weights_in, 16)
            sp.dma_start(w2[:], W_top2.rearrange("(k p) n -> p k n", p=P)).then_inc(weights_in, 16)
            sp.dma_start(h[:, :, PAIRS:K1], dense_v[:, 0, :, :]).then_inc(dense_in, 16)
            sp.sem_inc(y_row_free, 1)

            def load_idx(u, slot, row):
                for j in range(UNIT_TILES):
                    sp.wait_ge(rows_ready[slot * UNIT_TILES + j], ROWS_OF_TILE * row)
                    sp.dma_start(idx[:, slot * UNIT_TILES + j, :], ids_v[:, bass.ds(UNIT_TILES * u + j, 1), :]
                                 ).then_inc(idx_ready[slot * UNIT_TILES + j], 16)

            def load_dense(u):
                sp.wait_ge(w_filled, NW * (u - 1) + WORK_AT["H", KC - 1] + 1)
                sp.dma_start(h[:, :, PAIRS:K1], dense_v[:, bass.ds(u, 1), :, :]).then_inc(dense_in, 16)

            def store_y(u):
                sp.wait_ge(y_row_ready, u + 1)
                sp.dma_start(y_v[:, bass.ds(u, 1), :], y_row[:, :]).then_inc(y_out, 16)
                sp.wait_ge(y_out, 16 * (u + 1))
                sp.sem_inc(y_row_free, 1)

            with sp.Fori(1, UNITS // SLOTS) as k:
                for slot in range(SLOTS):
                    load_idx(SLOTS * k + slot, slot, k)
                    load_dense(SLOTS * (k - 1) + slot + 1)
                    store_y(SLOTS * (k - 1) + slot)
            for u in range(UNITS - SLOTS, UNITS):
                if u + 1 < UNITS:
                    load_dense(u + 1)
                store_y(u)

        @block.gpsimd
        def _(pool):
            nc.gpsimd.memset(ident[:], 0.0).then_inc(ident_zeroed, 1)
            pool.wait_ge(ident_zeroed, 1)
            nc.gpsimd.affine_select(out=ident[:], in_=ident[:], compare_op=ALU.not_equal, fill=1.0, base=0,
                                    pattern=[[-1, P]], channel_multiplier=1).then_inc(ident_ready, 1)
            nc.gpsimd.memset(et[:, :, :, NF:STRIP], 0.0).then_inc(pads_ready, 1)
            nc.gpsimd.iota(row_no_i[:], [[1, OC]], base=0, channel_multiplier=OC).then_inc(row_no_made, 1)
            with pool.Fori(0, UNITS // SLOTS) as k:
                for slot in range(SLOTS):
                    u = SLOTS * k + slot
                    for j in range(slot * UNIT_TILES, (slot + 1) * UNIT_TILES):
                        if j == TILES - 2:
                            pool.wait_ge(ids_float, 1)
                        if j == TILES - 1:
                            pool.wait_ge(lo_ready, NOH)
                            pool.wait_ge(hi_ready, NOH)
                        if j % UNIT_TILES == 0:
                            rnd, until = u - SLOTS - 1, len(E_STEPS)
                        else:
                            rnd, until = u - SLOTS, E_AT["T1", NT - 1] + 1
                        for bank in range(2):
                            pool.wait_ge(e_drained[bank], e_drains_before(rnd, until, bank))
                        pool.wait_ge(idx_ready[j], 16 * (k + 1))
                        pool.sem_inc(tile_started, 1)
                        for i, f in enumerate(GATHERED):
                            pool.indirect_dma_start(
                                rows[:, j, i, :], None, tables[f],
                                bass.IndirectOffsetOnAxis(ap=idx[:, j, f:f + 1], axis=0)
                            ).then_inc(rows_ready[j], 16)

        @block.tensor
        def _(pe):
            def free_e_bank(rnd, n):
                pe.wait_ge(e_drained[n % 2], e_drains_before(rnd, n, n % 2))

            def broadcast_ids(u, q):
                pe.sem_inc(broadcast_begun, 1)
                nc.tensor.matmul(id_bank[0:OP, :], ident_h[:, q:q + 1].broadcast_to([NOH, OP]),
                                 idsT[:, bass.ds(UNIT * u, UNIT)], start=True, stop=True).then_inc(ids_broadcast, 1)

            def look_up(rnd, q):
                u = rnd + 1
                n = E_AT["OH", q]
                free_e_bank(rnd, n)
                for piece in range(PIECES):
                    pe.wait_ge(one_hot_ready, PIECES * (NOH * u + q) + piece + 1)
                    if piece == PIECES - 1 and q + 1 < NOH:
                        broadcast_ids(u, q + 1)
                    for c in range(piece * PIECE, (piece + 1) * PIECE):
                        for part in (table_hi, table_lo):
                            last = nc.tensor.matmul(e_bank[n % 2][:, 0:UNIT], part[:, q, c, :],
                                                    one_hot[:, piece, c % PIECE, :],
                                                    start=(c == 0 and part is table_hi),
                                                    stop=(c == OC - 1 and part is table_lo))
                    last.then_inc(one_hot_used, 1)

            def transposes(rnd, slot, kind, i):
                n = E_AT[kind, i]
                j = slot * UNIT_TILES + 1 if kind == "T1" else (slot + 1) % SLOTS * UNIT_TILES
                free_e_bank(rnd, n)
                for a, f in enumerate(T_FEATS[i]):
                    last = nc.tensor.transpose(e_bank[n % 2][:, a * P:(a + 1) * P],
                                               rows[:, j, GATHERED.index(f), :], ident[:])
                last.then_inc(t_filled, 1)

            def grams(u, slot, q):
                for g in range(QUADS):
                    pe.wait_ge(g_drained[g], G_CHUNKS * u + q + 1)
                for i in range(2 * G_HALF):
                    b = (2 * G_HALF * q + i) * QUADS
                    four = et[:, slot, b:b + QUADS, :]
                    last = nc.tensor.matmul(g_banks[0:GROWS, i // G_HALF, i % G_HALF * GW:(i % G_HALF + 1) * GW],
                                            four.rearrange("p g f -> p (g f)")[:, 0:GROWS], four[:, :, 0:NF],
                                            start=True, stop=True)
                last.then_inc(g_filled, 1)

            def wait_drained(u, fills):
                for bank, n in {n % WB: n for n in sorted(fills)}.items():
                    pe.wait_ge(w_drained[bank], W_USES[bank] * u + n // WB + 2)

            def work(u, n):
                kind, i = WORK[n]
                bank = w_bank[n % WB]
                own = [n - WB] if n >= WB else []

                def operand(c, of):
                    wait_drained(u, (own if c == 0 else []) + ([WORK_AT[of, c]] if i == 0 else []))

                if n < WB:
                    pe.wait_ge(w_drained[n], W_USES[n] * u + 1)
                if kind == "H":
                    pe.wait_ge(pairs_packed, KC * u + i + 1)
                    if i == KC - 1:
                        pe.wait_ge(dense_in, 16 * (u + 1))
                if kind == "H":
                    for j in range(UNIT_TILES):
                        last = nc.tensor.transpose(bank[0:KROWS[i], j * P:(j + 1) * P],
                                                   h[:, j, i * P:i * P + KROWS[i]], ident[:])
                elif kind == "L1":
                    for c in range(KC):
                        operand(c, "H")
                        last = nc.tensor.matmul(bank[:, 0:UNIT], w1[0:KROWS[c], c, i * P:(i + 1) * P],
                                                hT[0:KROWS[c], c, :], start=(c == 0), stop=(c == KC - 1))
                elif kind == "L2":
                    for c in range(M1):
                        operand(c, "L1")
                        last = nc.tensor.matmul(bank[:, 0:UNIT], w2[:, c, i * P:(i + 1) * P], a1T[:, c, :],
                                                start=(c == 0), stop=(c == M1 - 1))
                else:
                    for c in range(M2):
                        operand(c, "L2")
                        last = nc.tensor.matmul(bank[0:1, 0:UNIT], w3[:, c:c + 1], a2T[:, c, :],
                                                start=(c == 0), stop=(c == M2 - 1))
                last.then_inc(w_filled, 1)

            def tile_gathered(j, turn):
                pe.wait_ge(rows_ready[j], ROWS_OF_TILE * (turn + 1))

            def round_of(u, slot, turn, turn_of_next):
                has_next = turn_of_next is not None
                for bank in range(2):
                    pe.wait_ge(e_drained[bank], e_drains_before(u, 0, bank))
                if has_next:
                    broadcast_ids(u + 1, 0)
                for kind, i in steps(has_next):
                    if kind == "G":
                        if i == G_TILE:
                            until = E_AT["T1", NT - 1] + 1
                            for bank in range(2):
                                pe.wait_ge(e_drained[bank], e_drains_before(u, until, bank))
                        grams(u, slot, i)
                    elif kind == "OH":
                        look_up(u, i)
                    elif kind == "T1":
                        if i == 0:
                            tile_gathered(slot * UNIT_TILES + 1, turn)
                        transposes(u, slot, kind, i)
                    elif kind == "T0":
                        if i == 0:
                            tile_gathered((slot + 1) % SLOTS * UNIT_TILES, turn_of_next)
                        transposes(u, slot, kind, i)
                    elif kind == "W":
                        work(u, i)

            pe.wait_ge(ident_ready, 1)
            pe.wait_ge(ids_float, 1)
            for t in range(B // P):
                if t % 4 == 0 and t >= 4 * WB:
                    pe.wait_ge(idsT_ready, t // 4 - WB + 1)
                last = nc.tensor.transpose(w_bank[t // 4 % WB][0:NOH, t % 4 * P:(t % 4 + 1) * P], ids_f[:, t, :], ident[:])
                if t % 4 == 3:
                    last.then_inc(ids_transposed, 1)
            pe.wait_ge(idsT_ready, B // BANK + 1)
            pe.wait_ge(vectors_in, 48)
            nc.tensor.transpose(w_bank[0][:, 0:NV], vec_rows[:], ident[0:NV, 0:NV]).then_inc(vectors_transposed, 1)
            pe.sem_inc(t_filled, NT)
            broadcast_ids(0, 0)
            for kind, i in FIRST_STEPS:
                if kind == "OH":
                    pe.wait_ge(hi_ready, i + 1)
                    pe.wait_ge(lo_ready, i + 1)
                    look_up(FIRST, i)
                else:
                    if i == 0:
                        tile_gathered(0, 0)
                    transposes(FIRST, SLOTS - 1, kind, i)
            pe.wait_ge(weights_in, 16 * WEIGHT_DMAS)
            pe.wait_ge(vectors_ready, 1)
            pe.wait_ge(pads_ready, 2)
            with pe.Fori(0, UNITS // SLOTS - 1) as k:
                round_of(SLOTS * k, 0, k, k)
                round_of(SLOTS * k + 1, 1, k, k + 1)
            round_of(UNITS - 2, 0, UNITS // SLOTS - 1, UNITS // SLOTS - 1)
            round_of(LAST, 1, UNITS // SLOTS - 1, None)

        @block.scalar
        def _(act):
            for bank in range(2):
                act.sem_inc(e_drained[bank], E_LEAD + e_missing(bank))
            for g in range(QUADS):
                act.sem_inc(g_drained[g], 1)
            act.sem_inc(one_hot_used, PIECES)

            def keep_upper(q):
                act.wait_ge(table_in[q % 2], 32 * (q // 2 + 1))
                nc.scalar.activation(table_hi[:, q, :, :], stage[q % 2], ACT.Copy).then_inc(hi_ready, 1)

            for q in range(SPLIT_LEAD):
                keep_upper(q)
            for kind, i in FIRST_STEPS:
                if kind == "OH" and i + SPLIT_LEAD < NOH:
                    keep_upper(i + SPLIT_LEAD)
                drain_e("act", act, FIRST, SLOTS - 1, kind, i)
            act.wait_ge(vectors_ready, 1)
            with act.Fori(0, UNITS // SLOTS - 1) as k:
                drain_steps("act", act, SLOTS * k, 0, True)
                drain_steps("act", act, SLOTS * k + 1, 1, True)
            drain_steps("act", act, UNITS - 2, 0, True)
            drain_steps("act", act, UNITS - 1, 1, False)

        @block.vector
        def _(dve):
            dve.wait_ge(ids_in, 16)
            for q, f in enumerate(ONE_HOT):
                last = nc.vector.tensor_copy(ids_f[:, :, q:q + 1], ids_i[:, :, f:f + 1])
            last.then_inc(ids_float, 1)
            dve.wait_ge(row_no_made, 1)
            nc.vector.tensor_copy(row_no[:], row_no_i[:])
            dve.wait_ge(ident_ready, 1)
            nc.vector.tensor_copy(ident_h[:], ident[0:NOH, 0:NOH])
            for i in range(B // BANK):
                dve.wait_ge(ids_transposed, i + 1)
                nc.vector.tensor_copy(idsT[:, i * BANK:(i + 1) * BANK], w_bank[i % WB][0:NOH, :]).then_inc(idsT_ready, 1)
            dve.wait_ge(idsT_ready, B // BANK)
            dve.sem_inc(idsT_ready, 1)
            for i in range(WB):
                dve.sem_inc(w_drained[i], 1)
            dve.wait_ge(vectors_transposed, 1)
            nc.vector.tensor_copy(vec_cols[:], w_bank[0][:, 0:NV]).then_inc(vectors_ready, 1)

            def keep_rest(q):
                dve.wait_ge(hi_ready, q + 1)
                nc.vector.tensor_tensor(table_lo[:, q, :, :], stage[q % 2], table_hi[:, q, :, :].bitcast(F32),
                                        ALU.subtract).then_inc(lo_ready, 1)

            for q in range(SPLIT_LEAD):
                keep_rest(q)
            make_one_hot(dve, 0, 0)
            for kind, i in FIRST_STEPS:
                drain_e("dve", dve, FIRST, SLOTS - 1, kind, i)
                if (kind, i) in MAKE_AFTER:
                    make_one_hot(dve, 0, MAKE_AFTER[kind, i])
                if kind == "OH" and i + SPLIT_LEAD < NOH:
                    keep_rest(i + SPLIT_LEAD)
            nc.vector.memset(z[:], 0.0).then_inc(pads_ready, 1)
            dve.wait_ge(vectors_ready, 1)
            with dve.Fori(0, UNITS // SLOTS - 1) as k:
                drain_steps("dve", dve, SLOTS * k, 0, True)
                drain_steps("dve", dve, SLOTS * k + 1, 1, True)
            drain_steps("dve", dve, UNITS - 2, 0, True)
            drain_steps("dve", dve, UNITS - 1, 1, False)


NAMES = (["dense_ctx", "ids"] + [f"tbl_{f}" for f in range(27)]
         + ["W_top1", "b_top1", "W_top2", "b_top2", "W_top3"])


def kernel(**inputs):
    import numpy as np
    import concourse.bacc as bacc
    from concourse.bass_utils import run_bass_kernel_spmd

    nc = bacc.Bacc("TRN2", target_bir_lowering=False, num_devices=1)
    arrays, aps = {}, {}
    for name in NAMES:
        a = np.ascontiguousarray(inputs[name])
        arrays["in_" + name] = a
        aps[name] = nc.dram_tensor("in_" + name, a.shape, mybir.dt.from_np(a.dtype), kind="ExternalInput").ap()
    out = nc.dram_tensor("out_y", (inputs["ids"].shape[0], 1), F32, kind="ExternalOutput").ap()
    tables = [aps[n] for n in NAMES if n.startswith("tbl_")]
    dlrm_tower(nc, aps["dense_ctx"], aps["ids"], tables, aps["W_top1"], aps["b_top1"], aps["W_top2"],
               aps["b_top2"], aps["W_top3"], out)
    result = run_bass_kernel_spmd(nc, [arrays], core_ids=[0])
    return result.results[0]["out_y"]
```

```python
from contextlib import ExitStack

import concourse.bass as bass
from concourse import mybir

F32 = mybir.dt.float32
F32R = mybir.dt.float32r
F16 = mybir.dt.float16
I32 = mybir.dt.int32
ALU = mybir.AluOpType
ACT = mybir.ActivationFunctionType

P = 128
UNIT_TILES = 2
UNIT = UNIT_TILES * P
SLOTS = 2
STRIP = 32
QUADS = P // STRIP
BANK = 512
ONE_HOT = (14, 19, 22, 23, 24, 25, 26)
PIECE = 4


def dlrm_tower(nc, dense_ctx, ids, tables, W_top1, b_top1, W_top2, b_top2, W_top3, y):
    B, NF = ids.shape
    ND = dense_ctx.shape[1]
    D = tables[0].shape[1]
    K1, N1 = W_top1.shape
    N2 = W_top2.shape[1]
    PAIRS = NF * (NF - 1) // 2
    UNITS = B // UNIT
    assert PAIRS > (K1 - 1) // P * P
    assert D == P and K1 == PAIRS + ND and N1 % P == 0 and N2 <= PAIRS and NF <= STRIP
    assert B % (SLOTS * UNIT) == 0

    OC = 8
    V = tables[ONE_HOT[0]].shape[0]
    OP = V // OC
    assert all(tables[f].shape[0] == V for f in ONE_HOT) and OP * OC == V and OP <= P and OC % PIECE == 0
    assert OP % 16
    assert V <= 2048
    NOH = len(ONE_HOT)
    PIECES = OC // PIECE
    AGAIN = 3

    T_RUNS = [[range(0, 4)], [range(4, 8)], [range(8, 12)], [range(12, 14), range(20, 22)], [range(15, 19)]]
    T_FEATS = [[f for run in runs for f in run] for runs in T_RUNS]
    GATHERED = [f for feats in T_FEATS for f in feats]
    NG = len(GATHERED)
    assert sorted(GATHERED + list(ONE_HOT)) == list(range(NF)) and max(map(len, T_FEATS)) <= BANK // P
    NT = len(T_FEATS)

    GROUPS = UNIT // QUADS
    G_CHUNKS = 8
    G_TILE = G_CHUNKS // UNIT_TILES
    G_HALF = GROUPS // G_CHUNKS // 2
    NP = NF - 1
    GW = QUADS * NP
    GROWS = (QUADS - 1) * STRIP + NP
    assert NOH == 7 and G_TILE == 4 and NT == 5
    assert G_HALF * 2 * G_CHUNKS == GROUPS and G_HALF * GW <= BANK

    M1 = N1 // P
    KC = -(-K1 // P)
    KROWS = [min(P, K1 - c * P) for c in range(KC)]
    BOTH = tuple(range(UNIT_TILES))
    WORK = ([("H", c, BOTH) for c in range(KC)] + [("L1", m, BOTH) for m in range(M1)]
            + [("L2", j, (j,)) for j in range(UNIT_TILES)])
    LAST_WORK = []
    for j in range(UNIT_TILES):
        LAST_WORK += [("H", c, (j,)) for c in range(KC)] + [("L1", m, (j,)) for m in range(M1)] + [("L2", j, (j,))]
    NW = len(WORK)
    WB = 3
    W_USES = [len(range(bank, NW, WB)) for bank in range(WB)]

    ids_v = ids.rearrange("(t p) f -> p t f", p=P)
    dense_v = dense_ctx.rearrange("(u j p) c -> p u j c", j=UNIT_TILES, p=P)
    y_v = y.rearrange("(t p) o -> t (p o)", p=P)

    with ExitStack() as ctx:
        def sb(name, shape, dt=F32):
            return ctx.enter_context(nc.sbuf_tensor(name, shape, dt))

        def psum(name, shape):
            return ctx.enter_context(nc.psum_tensor(name, shape, F32))

        def sem(name):
            return ctx.enter_context(nc.semaphore(name))

        TILES = SLOTS * UNIT_TILES
        idx = sb("idx", [P, TILES, NF], I32)
        rows = sb("rows", [P, TILES, NG, D])
        et = sb("et", [P, SLOTS, UNIT, STRIP])
        z = sb("z", [P, GROUPS, NP])
        zt = sb("zt", [P, UNIT_TILES, NP, STRIP])
        h = sb("h", [P, UNIT_TILES, K1])
        hT = z[:].rearrange("p (j s) n -> p j (s n)", j=UNIT_TILES)[:, :, 0:KC * P] \
            .rearrange("p j (c b) -> p c j b", c=KC)
        a1T = zt[:].rearrange("p j n m -> p j (n m)")[:, :, 0:M1 * P] \
            .rearrange("p j (m b) -> p m j b", m=M1)
        a2 = h[:, :, 0:N2]
        y_cols = sb("y_cols", [P, B // P])
        w1 = sb("w1", [P, KC, N1])
        w2 = sb("w2", [P, M1, N2])
        b2_all = sb("b2_all", [P, N2])
        w3_all = sb("w3_all", [P, N2])
        row_buffer = sb("row_buffer", [B // P, P])
        b1_rows, y_rows = row_buffer[0:M1, :], row_buffer[:, :]
        b1 = sb("b1", [P, M1])
        ident = sb("ident", [P, P])
        ident_h = sb("ident_h", [NOH, NOH], F16)
        row_no_i = sb("row_no_i", [OP, OC], I32)
        row_no = sb("row_no", [OP, OC])
        table_hi = sb("table_hi", [OP, NOH, OC, D], F32R)
        table_lo = sb("table_lo", [OP, NOH, OC, D], F32R)
        one_hot = sb("one_hot", [OP, PIECES, PIECE, UNIT], F32R)
        idsT = sb("idsT", [NOH, B], F16)
        STAGES = ((TILES - 3, 0), (TILES - 3, OC), (TILES - 2, 4), (TILES - 1, 0), (TILES - 1, OC))
        stage = [rows[0:OP, j, i:i + OC, :] for j, i in STAGES]
        STAGE_OF = [q if q < len(STAGES) else q - AGAIN for q in range(NOH)]
        ids_i = rows[:, TILES - 2, 0:4, :].rearrange("p a d -> p (a d)").bitcast(I32)[:, 0:B // P * NF] \
            .rearrange("p (t f) -> p t f", f=NF)
        ids_f = zt[:].rearrange("p j n m -> p (j n m)")[:, 0:B // P * NOH].rearrange("p (t f) -> p t f", f=NOH)

        e_bank = [psum(f"e_bank{i}", [P, BANK]) for i in range(2)]
        id_bank = psum("id_bank", [P, UNIT])
        g_banks = psum("g_banks", [P, 2, BANK])
        w_bank = [psum(f"w_bank{i}", [P, BANK]) for i in range(WB)]

        weights_in = sem("weights_in")
        b1_rows_in = sem("b1_rows_in")
        b1_transposed = sem("b1_transposed")
        b1_ready = sem("b1_ready")
        y_weights_in = sem("y_weights_in")
        ident_zeroed = sem("ident_zeroed")
        ident_ready = sem("ident_ready")
        row_no_made = sem("row_no_made")
        pads_ready = sem("pads_ready")
        ids_in = sem("ids_in")
        ids_float = sem("ids_float")
        ids_transposed = sem("ids_transposed")
        idsT_ready = sem("idsT_ready")
        ident_h_ready = sem("ident_h_ready")
        table_in = [sem(f"table_in{i}") for i in range(len(STAGES))]
        hi_ready = sem("hi_ready")
        lo_ready = sem("lo_ready")
        idx_ready = [sem(f"idx_ready{j}") for j in range(TILES)]
        tile_started = sem("tile_started")
        rows_ready = [[sem(f"rows_ready{j}_{i}") for i in range(NT)] for j in range(TILES)]
        broadcast_begun = sem("broadcast_begun")
        ids_broadcast = sem("ids_broadcast")
        one_hot_ready = sem("one_hot_ready")
        one_hot_used = sem("one_hot_used")
        t_filled = sem("t_filled")
        e_drained = [sem(f"e_drained{i}") for i in range(2)]
        g_filled = sem("g_filled")
        g_drained = [sem(f"g_drained{q}") for q in range(QUADS)]
        z_turned = sem("z_turned")
        first_pairs_packed = sem("first_pairs_packed")
        later_pairs_packed = sem("later_pairs_packed")
        w_filled = sem("w_filled")
        w_drained = [sem(f"w_drained{i}") for i in range(WB)]
        dense_in = sem("dense_in")
        bias_added = sem("bias_added")
        y_ready = sem("y_ready")
        y_transposed = sem("y_transposed")
        y_rows_ready = sem("y_rows_ready")
        y_out = sem("y_out")

        WEIGHT_DMAS = KC + 1
        SPLIT_LEAD = 2

        def rows_landed(i, turns):
            return 16 * len(T_FEATS[i]) * turns

        def steps(has_next, has_second):
            def work(kind, tile=None):
                return [("W", n) for n, w in enumerate(WORK if has_next else LAST_WORK)
                        if w[0] == kind and (tile is None or w[2] == (tile,))]

            if not has_next:
                out = [("G", q) for q in range(G_TILE)] + [("T1", i) for i in range(NT - 2)]
                out += [("turn", 0), ("pack", 0), ("T1", NT - 2)]
                out += work("H", 0) + work("L1", 0)[:2] + [("T1", NT - 1)] + work("L1", 0)[2:3]
                out += [("G", q) for q in range(G_TILE, G_CHUNKS)] + [("turn", 1)]
                out += work("L1", 0)[3:] + [("pack", 1)] + work("L2", 0)
                return out + work("H", 1) + work("L1", 1) + work("L2", 1)

            out = [("G", 0), ("OH", 0)]
            out += [("G", 1), ("T1", 0), ("OH", 1), ("T1", 1)]
            out += [("G", 2), ("T1", 2), ("OH", 2), ("T1", 3)]
            out += [("G", 3), ("T1", 4), ("OH", 3)]
            out += [("G", 4), ("OH", 4), ("turn", 0)]
            out += [("G", 5), ("OH", 5)]
            out += [("G", 6), ("T0", 0), ("T0", 1), ("pack", 0)]
            out += [("G", 7), ("T0", 2), ("turn", 1), ("pack", 1), ("OH", 6), ("T0", 3)]
            out += [("H", 0), ("H", 1)] + work("H") + [("T0", 4)] + work("L1")
            return out + ([("ids", 0)] if has_second else []) + work("L2")

        MAKE_AFTER = {("OH", q - 1): q for q in range(1, NOH)}

        E_STEPS = [s for s in steps(True, True) if s[0] in ("OH", "T0", "T1")]
        FIRST_STEPS = [s for s in E_STEPS if s[0] != "T1"]
        E_AT = {s: n for n, s in enumerate(E_STEPS)}
        LAST_AT = {("T1", i): i for i in range(NT)}
        FIRST, LAST = -1, UNITS - 1
        E_USES = [len(range(bank, len(E_STEPS), 2)) for bank in range(2)]

        def e_missing(bank):
            return len([n for s, n in E_AT.items() if s[0] == "T1" and n % 2 == bank])

        def e_lead(bank):
            return 2 * E_USES[bank]

        def e_number(rnd, kind, i):
            return (LAST_AT if rnd is LAST else E_AT)[kind, i]

        def e_drains_before(rnd, n, bank):
            earlier = [s for s, m in (LAST_AT if rnd is LAST else E_AT).items() if m < n and m % 2 == bank]
            if rnd is FIRST:
                earlier = [s for s in earlier if s[0] != "T1"] + [None] * e_missing(bank)
            return e_lead(bank) + E_USES[bank] * (rnd + 1) + len(earlier)

        def t_fills_until(rnd, kind, i):
            return 2 * NT * (rnd + 1) + (NT if kind == "T0" else 0) + i + 1

        def g_engine(q, g, last):
            if last or q >= G_CHUNKS - 2:
                return "act" if g < 2 else "dve"
            return "act" if g < 3 else "dve"

        def w_engine(n, last):
            kind, i, tiles = (LAST_WORK if last else WORK)[n]
            if kind == "L2":
                return "dve"
            if last and (kind == "H" or tiles == (0,)):
                return "act"
            return "act" if i % 2 == 0 else "dve"

        def e_engine(rnd, kind, i):
            return "dve" if (kind, i) == ("OH", NOH - 1) or rnd is LAST and i == NT - 2 else "act"

        def copy(eng, out, src):
            if eng == "act":
                return nc.scalar.activation(out, src, ACT.Copy)
            return nc.vector.tensor_copy(out, src)

        def drain_e(me, engine, rnd, slot, kind, i):
            if e_engine(rnd, kind, i) != me:
                return
            n = e_number(rnd, kind, i)
            bank = e_bank[n % 2]
            if kind == "OH":
                engine.wait_ge(one_hot_used, PIECES * (NOH * (rnd + 1) + i + 1) + PIECES)
                out = et[:, (slot + 1) % SLOTS, :, ONE_HOT[i]].rearrange("p (j s g) -> p j s g", g=QUADS, s=STRIP)
                src = bank[:, 0:UNIT].rearrange("p (j g s) -> p j s g", g=QUADS, s=STRIP)
            else:
                engine.wait_ge(t_filled, t_fills_until(rnd, kind, i))
                to, j = (slot, 1) if kind == "T1" else ((slot + 1) % SLOTS, 0)
                a = 0
                for run in T_RUNS[i]:
                    out = et[:, to, j * P:(j + 1) * P, run[0]:run[-1] + 1:run.step]
                    src = bank[:, a * P:(a + len(run)) * P].rearrange("p (f g s) -> p s g f", g=QUADS, s=STRIP)
                    last = copy(me, out.rearrange("p (s g) f -> p s g f", g=QUADS), src)
                    a += len(run)
                last.then_inc(e_drained[n % 2], 1)
                return
            copy(me, out, src).then_inc(e_drained[n % 2], 1)

        def g_fills_until(u, q, bank, last):
            return G_CHUNKS * u + (2 * q + bank + 1 if last else q + 1)

        def g_drains_before(u, q, bank, last):
            return G_CHUNKS * u + (max(2 * q + bank, 1) if last else q + 1)

        def drain_g(me, engine, u, q, last):
            for banks in ((0, 1), (1, 2)) if last else ((0, 2),):
                engine.wait_ge(g_filled, g_fills_until(u, q, banks[0], last))
                for g in range(QUADS):
                    if g_engine(q, g, last) != me:
                        continue
                    strip = slice(g * STRIP, g * STRIP + NP)
                    src = g_banks[strip, banks[0]:banks[1], 0:G_HALF * GW].rearrange("p k (s c) -> p k s c", c=GW)
                    at = 2 * q + banks[0]
                    out = z[strip, G_HALF * at:G_HALF * (at + banks[1] - banks[0]), :]
                    copy(me, out.rearrange("p (k s) n -> p k s n", s=G_HALF), src[:, :, :, g * NP:(g + 1) * NP]
                         ).then_inc(g_drained[g], 1)

        def drain_w(me, engine, u, n, last):
            kind, i, tiles = (LAST_WORK if last else WORK)[n]
            if w_engine(n, last) != me:
                return
            engine.wait_ge(w_filled, NW * u + n + 1)
            bank, done = w_bank[n % WB], w_drained[n % WB]
            cols = bank[:, 0:len(tiles) * P].rearrange("p (j b) -> p j b", b=P)
            if kind == "H":
                copy(me, hT[0:KROWS[i], i, tiles[0]:tiles[-1] + 1, :], cols[0:KROWS[i]]).then_inc(done, 1)
            elif kind == "L1":
                out = a1T[:, i, tiles[0]:tiles[-1] + 1, :]
                if me == "act":
                    nc.scalar.activation(out, cols, ACT.Relu, bias=b1[:, i:i + 1]).then_inc(done, 1)
                else:
                    nc.vector.tensor_scalar(out, cols, b1[:, i:i + 1], 0.0, ALU.add, ALU.max).then_inc(done, 1)
            else:
                nc.vector.tensor_tensor(a2[:, i, :], bank[:, 0:N2], b2_all[:], ALU.add).then_inc(done, 1)
                engine.wait_ge(done, W_USES[n % WB] * u + n // WB + 2)
                engine.sem_inc(bias_added, 1)
                nc.vector.scalar_tensor_tensor(a2[:, i, :], a2[:, i, :], 0.0, w3_all[:], ALU.max, ALU.mult,
                                               accum_out=y_cols[:, bass.ds(UNIT_TILES * u + i, 1)]
                                               ).then_inc(y_ready, 1)

        def turn_tile(dve, u, j, last):
            for g in range(QUADS):
                dve.wait_ge(g_drained[g], G_CHUNKS * u + (j + 1) * G_TILE * (2 if last else 1) + 1)
            if j == 0:
                dve.wait_ge(y_ready, UNIT_TILES * u + 1)
            nc.vector.transpose(zt[:, j, :, :], z[:, j * STRIP:(j + 1) * STRIP, :].rearrange("p s n -> p n s")
                                ).then_inc(z_turned, 1)

        def pack_pairs(me, engine, u, j):
            engine.wait_ge(z_turned, UNIT_TILES * u + j + 1)
            chunk = 1
            for n in range(1, NF):
                first = n * (n - 1) // 2
                if (me == "dve") != (first < P):
                    continue
                last = copy(me, h[:, j, first:first + n], zt[:, j, n - 1, 0:n])
                if me == "act" and first + n >= min((chunk + 1) * P, PAIRS):
                    last.then_inc(later_pairs_packed, 1)
                    chunk += 1
            if me == "dve":
                last.then_inc(first_pairs_packed, 1)
            else:
                assert chunk == KC

        def drain_steps(me, engine, u, slot, has_next, has_second):
            for kind, i in steps(has_next, has_second):
                if kind == "G":
                    drain_g(me, engine, u, i, not has_next)
                elif kind == "turn" and me == "dve":
                    turn_tile(engine, u, i, not has_next)
                elif kind == "pack":
                    pack_pairs(me, engine, u, i)
                elif kind == "W":
                    drain_w(me, engine, u, i, not has_next)
                elif kind in ("OH", "T0", "T1"):
                    drain_e(me, engine, u, slot, kind, i)
                elif kind == "ids" and me == "dve":
                    make_one_hot(engine, u + 2, 0)
                if me == "dve" and (kind, i) in MAKE_AFTER and has_next:
                    make_one_hot(engine, u + 1, MAKE_AFTER[kind, i])

        def make_one_hot(dve, u, q):
            for piece in range(PIECES):
                if piece == 0:
                    dve.wait_ge(ids_broadcast, NOH * u + q + 1)
                dve.wait_ge(one_hot_used, PIECES * (NOH * u + q) + piece + 1)
                nc.vector.tensor_tensor(
                    one_hot[:, piece, :, :],
                    id_bank[0:OP, :].unsqueeze(1).broadcast_to([OP, PIECE, UNIT]),
                    row_no[:, piece * PIECE:(piece + 1) * PIECE].unsqueeze(2).broadcast_to([OP, PIECE, UNIT]),
                    ALU.is_equal).then_inc(one_hot_ready, 1)

        block = ctx.enter_context(nc.Block())

        @block.sync
        def _(sp):
            def load_table(q):
                place = STAGE_OF[q]
                if q >= len(STAGES):
                    sp.wait_ge(lo_ready, q - AGAIN + 1)
                table = tables[ONE_HOT[q]].rearrange("(p c) d -> p c d", c=OC)
                for part in (slice(0, OP // 16 * 16), slice(OP // 16 * 16, OP)):
                    sp.dma_start(stage[place][part], table[part]).then_inc(table_in[place], 16)

            sp.dma_start(idx[:, 0, :], ids_v[:, 0, :]).then_inc(idx_ready[0], 16)
            sp.dma_start(ids_i, ids_v).then_inc(ids_in, 16)
            load_table(0)
            load_table(1)
            for j in range(1, TILES):
                sp.dma_start(idx[:, j, :], ids_v[:, j, :]).then_inc(idx_ready[j], 16)
            for q in range(2, len(STAGES)):
                load_table(q)
            sp.dma_start(b1_rows, b_top1.rearrange("(m p) -> m p", p=P)).then_inc(b1_rows_in, 16)
            sp.dma_start(b2_all[:], b_top2.rearrange("(o n) -> o n", o=1).broadcast_to([P, N2])
                         ).then_inc(y_weights_in, 16)
            sp.dma_start(w3_all[:], W_top3.rearrange("n o -> o n").broadcast_to([P, N2])
                         ).then_inc(y_weights_in, 16)
            for q in range(len(STAGES), NOH):
                load_table(q)
            for c in range(KC):
                sp.dma_start(w1[0:KROWS[c], c, :], W_top1[c * P:c * P + KROWS[c], :]).then_inc(weights_in, 16)
            sp.dma_start(w2[:], W_top2.rearrange("(k p) n -> p k n", p=P)).then_inc(weights_in, 16)
            sp.dma_start(h[:, :, PAIRS:K1], dense_v[:, 0, :, :]).then_inc(dense_in, 16)

            def load_idx(u, slot, row):
                for j in range(UNIT_TILES):
                    for i in range(NT):
                        sp.wait_ge(rows_ready[slot * UNIT_TILES + j][i], rows_landed(i, row))
                    sp.dma_start(idx[:, slot * UNIT_TILES + j, :], ids_v[:, bass.ds(UNIT_TILES * u + j, 1), :]
                                 ).then_inc(idx_ready[slot * UNIT_TILES + j], 16)

            def load_dense(u):
                sp.wait_ge(w_filled, NW * (u - 1) + WORK.index(("H", KC - 1, BOTH)) + 1)
                sp.dma_start(h[:, :, PAIRS:K1], dense_v[:, bass.ds(u, 1), :, :]).then_inc(dense_in, 16)

            with sp.Fori(1, UNITS // SLOTS) as k:
                for slot in range(SLOTS):
                    load_idx(SLOTS * k + slot, slot, k)
                    load_dense(SLOTS * (k - 1) + slot + 1)
            for u in range(UNITS - SLOTS, UNITS - 1):
                load_dense(u + 1)
            sp.wait_ge(y_rows_ready, 1)
            sp.dma_start(y_v, y_rows).then_inc(y_out, 16)
            sp.wait_ge(y_out, 16)

        @block.gpsimd
        def _(pool):
            nc.gpsimd.memset(ident[:], 0.0).then_inc(ident_zeroed, 1)
            pool.wait_ge(ident_zeroed, 1)
            nc.gpsimd.affine_select(out=ident[:], in_=ident[:], compare_op=ALU.not_equal, fill=1.0, base=0,
                                    pattern=[[-1, P]], channel_multiplier=1).then_inc(ident_ready, 1)
            nc.gpsimd.iota(row_no_i[:], [[1, OC]], base=0, channel_multiplier=OC).then_inc(row_no_made, 1)
            with pool.Fori(0, UNITS // SLOTS) as k:
                for slot in range(SLOTS):
                    u = SLOTS * k + slot
                    for j in range(slot * UNIT_TILES, (slot + 1) * UNIT_TILES):
                        if j == TILES - 2:
                            pool.wait_ge(ids_float, 1)
                        staged = [q for q in range(NOH) if STAGES[STAGE_OF[q]][0] == j]
                        if staged:
                            pool.wait_ge(lo_ready, staged[-1] + 1)
                            pool.wait_ge(hi_ready, staged[-1] + 1)
                        if j % UNIT_TILES == 0:
                            rnd, until = u - SLOTS - 1, len(E_STEPS)
                        else:
                            rnd, until = u - SLOTS, E_AT["T1", NT - 1] + 1
                        for bank in range(2):
                            pool.wait_ge(e_drained[bank], e_drains_before(rnd, until, bank))
                        pool.wait_ge(idx_ready[j], 16 * (k + 1))
                        pool.sem_inc(tile_started, 1)
                        for i, f in enumerate(GATHERED):
                            pool.indirect_dma_start(
                                rows[:, j, i, :], None, tables[f],
                                bass.IndirectOffsetOnAxis(ap=idx[:, j, f:f + 1], axis=0)
                            ).then_inc(rows_ready[j][[f in feats for feats in T_FEATS].index(True)], 16)

        @block.tensor
        def _(pe):
            def free_e_bank(rnd, n):
                pe.wait_ge(e_drained[n % 2], e_drains_before(rnd, n, n % 2))

            def broadcast_ids(u, q):
                pe.sem_inc(broadcast_begun, 1)
                nc.tensor.matmul(id_bank[0:OP, :], ident_h[:, q:q + 1].broadcast_to([NOH, OP]),
                                 idsT[:, bass.ds(UNIT * u, UNIT)], start=True, stop=True).then_inc(ids_broadcast, 1)

            def look_up(rnd, q):
                u = rnd + 1
                n = e_number(rnd, "OH", q)
                free_e_bank(rnd, n)
                for piece in range(PIECES):
                    pe.wait_ge(one_hot_ready, PIECES * (NOH * u + q) + piece + 1)
                    if piece == PIECES - 1 and q + 1 < NOH:
                        broadcast_ids(u, q + 1)
                    for c in range(piece * PIECE, (piece + 1) * PIECE):
                        for part in (table_hi, table_lo):
                            last = nc.tensor.matmul(e_bank[n % 2][:, 0:UNIT], part[:, q, c, :],
                                                    one_hot[:, piece, c % PIECE, :],
                                                    start=(c == 0 and part is table_hi),
                                                    stop=(c == OC - 1 and part is table_lo))
                    last.then_inc(one_hot_used, 1)

            def transposes(rnd, slot, kind, i, turn):
                n = e_number(rnd, kind, i)
                j = slot * UNIT_TILES + 1 if kind == "T1" else (slot + 1) % SLOTS * UNIT_TILES
                free_e_bank(rnd, n)
                pe.wait_ge(rows_ready[j][i], rows_landed(i, turn + 1))
                for a, f in enumerate(T_FEATS[i]):
                    last = nc.tensor.transpose(e_bank[n % 2][:, a * P:(a + 1) * P],
                                               rows[:, j, GATHERED.index(f), :], ident[:])
                last.then_inc(t_filled, 1)

            def grams(u, slot, q, last_round):
                for i in range(2 * G_HALF):
                    if i == 0 or i == G_HALF and last_round:
                        for g in range(QUADS):
                            pe.wait_ge(g_drained[g], g_drains_before(u, q, i // G_HALF, last_round))
                    b = (2 * G_HALF * q + i) * QUADS
                    four = et[:, slot, b:b + QUADS, :]
                    last = nc.tensor.matmul(g_banks[0:GROWS, i // G_HALF, i % G_HALF * GW:(i % G_HALF + 1) * GW],
                                            four.rearrange("p g f -> p (g f)")[:, 0:GROWS], four[:, :, 1:NF],
                                            start=True, stop=True)
                    if i == 2 * G_HALF - 1 or i == G_HALF - 1 and last_round:
                        last.then_inc(g_filled, 1)

            def wait_drained(u, fills):
                for bank, n in {n % WB: n for n in sorted(fills)}.items():
                    pe.wait_ge(w_drained[bank], W_USES[bank] * u + n // WB + 2)

            def work(u, n, last_round):
                items = LAST_WORK if last_round else WORK
                kind, i, tiles = items[n]
                bank = w_bank[n % WB]
                own = [n - WB] if n >= WB else []
                if n < WB:
                    pe.wait_ge(w_drained[n], W_USES[n] * u + 1)

                def operand(c, of, of_tiles):
                    wait_drained(u, (own if c == 0 else [])
                                 + ([items.index((of, c, of_tiles))] if i == 0 or len(of_tiles) == 1 else []))

                if kind == "H":
                    (j,) = tiles
                    wait_drained(u, own)
                    wait_packed(u, j, i)
                    last = nc.tensor.transpose(bank[0:KROWS[i], 0:P], h[:, j, i * P:i * P + KROWS[i]], ident[:])
                elif kind == "L1":
                    for c in range(KC):
                        operand(c, "H", tiles)
                        last = nc.tensor.matmul(bank[:, 0:len(tiles) * P], w1[0:KROWS[c], c, i * P:(i + 1) * P],
                                                hT[0:KROWS[c], c, tiles[0]:tiles[-1] + 1, :],
                                                start=(c == 0), stop=(c == KC - 1))
                else:
                    for c in range(M1):
                        operand(c, "L1", (i,) if last_round else BOTH)
                        last = nc.tensor.matmul(bank[:, 0:N2], a1T[:, c, i, :], w2[:, c, :],
                                                start=(c == 0), stop=(c == M1 - 1))
                last.then_inc(w_filled, 1)

            def wait_packed(u, j, c):
                if c < 2:
                    pe.wait_ge(first_pairs_packed, UNIT_TILES * u + j + 1)
                if c > 0:
                    pe.wait_ge(later_pairs_packed, (KC - 1) * (UNIT_TILES * u + j) + c)
                if c == KC - 1:
                    pe.wait_ge(dense_in, 16 * (u + 1))

            def turn_h(u, j):
                for c in range(KC):
                    if j == 0:
                        pe.wait_ge(w_drained[c], W_USES[c] * u + 1)
                    wait_packed(u, j, c)
                    last = nc.tensor.transpose(w_bank[c][0:KROWS[c], j * P:(j + 1) * P],
                                               h[:, j, c * P:c * P + KROWS[c]], ident[:])
                    if j == UNIT_TILES - 1:
                        last.then_inc(w_filled, 1)

            def round_of(u, slot, turn, turn_of_next, has_second):
                has_next = turn_of_next is not None
                for bank in range(2):
                    pe.wait_ge(e_drained[bank], e_drains_before(u, 0, bank))
                for kind, i in steps(has_next, has_second):
                    if kind == "G":
                        if i == G_TILE:
                            until = e_number(u, "T1", NT - 1) + 1
                            for bank in range(2):
                                pe.wait_ge(e_drained[bank], e_drains_before(u, until, bank))
                        grams(u, slot, i, not has_next)
                    elif kind == "OH":
                        look_up(u, i)
                    elif kind == "T1":
                        transposes(u, slot, kind, i, turn)
                    elif kind == "T0":
                        transposes(u, slot, kind, i, turn_of_next)
                    elif kind == "H":
                        turn_h(u, i)
                    elif kind == "ids":
                        broadcast_ids(u + 2, i)
                    elif kind == "W" and (not has_next or WORK[i][0] != "H"):
                        work(u, i, not has_next)

            pe.wait_ge(ident_ready, 1)
            pe.wait_ge(ids_float, 1)
            for t in range(B // P):
                if t == 4:
                    pe.wait_ge(ident_h_ready, 1)
                    pe.wait_ge(idsT_ready, 1)
                    broadcast_ids(0, 0)
                if t % 4 == 0 and t >= 4 * WB:
                    pe.wait_ge(idsT_ready, t // 4 - WB + 1)
                last = nc.tensor.transpose(w_bank[t // 4 % WB][0:NOH, t % 4 * P:(t % 4 + 1) * P],
                                           ids_f[:, t, :], ident[:])
                if t % 4 == 3:
                    last.then_inc(ids_transposed, 1)
            pe.sem_inc(t_filled, NT)
            for kind, i in FIRST_STEPS:
                if kind == "OH":
                    pe.wait_ge(hi_ready, i + 1)
                    pe.wait_ge(lo_ready, i + 1)
                    look_up(FIRST, i)
                else:
                    transposes(FIRST, SLOTS - 1, kind, i, 0)
            pe.wait_ge(idsT_ready, B // BANK)
            broadcast_ids(1, 0)
            pe.wait_ge(b1_rows_in, 16)
            nc.tensor.transpose(w_bank[0][:, 0:M1], b1_rows, ident[0:M1, 0:M1]).then_inc(b1_transposed, 1)
            pe.wait_ge(weights_in, 16 * WEIGHT_DMAS)
            pe.wait_ge(b1_ready, 1)
            pe.wait_ge(pads_ready, 3)
            with pe.Fori(0, UNITS // SLOTS - 1) as k:
                round_of(SLOTS * k, 0, k, k, True)
                round_of(SLOTS * k + 1, 1, k, k + 1, True)
            round_of(UNITS - 2, 0, UNITS // SLOTS - 1, UNITS // SLOTS - 1, False)
            round_of(LAST, 1, UNITS // SLOTS - 1, None, False)
            pe.wait_ge(y_ready, UNITS * UNIT_TILES + 1)
            nc.tensor.transpose(w_bank[0][0:B // P, 0:P], y_cols[:], ident[:]).then_inc(y_transposed, 1)

        @block.scalar
        def _(act):
            for bank in range(2):
                act.sem_inc(e_drained[bank], e_lead(bank) + e_missing(bank))
            for g in range(QUADS):
                act.sem_inc(g_drained[g], 1)
            act.sem_inc(one_hot_used, PIECES)

            def keep_upper(q):
                act.wait_ge(table_in[STAGE_OF[q]], 32 if q < len(STAGES) else 64)
                nc.scalar.activation(table_hi[:, q, :, :], stage[STAGE_OF[q]], ACT.Copy).then_inc(hi_ready, 1)

            keep_upper(0)
            for i in range(B // BANK):
                if 0 < i < SPLIT_LEAD:
                    keep_upper(i)
                act.wait_ge(ids_transposed, i + 1)
                nc.scalar.activation(idsT[:, i * BANK:(i + 1) * BANK], w_bank[i % WB][0:NOH, :], ACT.Copy
                                     ).then_inc(idsT_ready, 1)
            for kind, i in FIRST_STEPS:
                if kind == "OH" and i + SPLIT_LEAD < NOH:
                    keep_upper(i + SPLIT_LEAD)
                drain_e("act", act, FIRST, SLOTS - 1, kind, i)
            act.wait_ge(b1_transposed, 1)
            nc.scalar.activation(b1[:], w_bank[0][:, 0:M1], ACT.Copy).then_inc(b1_ready, 1)
            act.wait_ge(b1_ready, 1)
            for i in range(WB):
                act.sem_inc(w_drained[i], 1)
            with act.Fori(0, UNITS // SLOTS - 1) as k:
                drain_steps("act", act, SLOTS * k, 0, True, True)
                drain_steps("act", act, SLOTS * k + 1, 1, True, True)
            drain_steps("act", act, UNITS - 2, 0, True, False)
            drain_steps("act", act, LAST, 1, False, False)
            act.wait_ge(y_transposed, 1)
            nc.scalar.activation(y_rows, w_bank[0][0:B // P, 0:P], ACT.Copy).then_inc(y_rows_ready, 1)

        @block.vector
        def _(dve):
            nc.vector.memset(z[:], 0.0).then_inc(pads_ready, 1)
            nc.vector.memset(et[:, 0, :, NF:STRIP], 0.0).then_inc(pads_ready, 1)
            dve.wait_ge(ids_in, 16)
            for q, f in enumerate(ONE_HOT):
                last = nc.vector.tensor_copy(ids_f[:, :, q:q + 1], ids_i[:, :, f:f + 1])
            last.then_inc(ids_float, 1)
            dve.wait_ge(row_no_made, 1)
            nc.vector.tensor_copy(row_no[:], row_no_i[:])
            dve.wait_ge(ident_ready, 1)
            nc.vector.tensor_copy(ident_h[:], ident[0:NOH, 0:NOH]).then_inc(ident_h_ready, 1)

            def keep_rest(q):
                dve.wait_ge(hi_ready, q + 1)
                nc.vector.tensor_tensor(table_lo[:, q, :, :], stage[STAGE_OF[q]], table_hi[:, q, :, :].bitcast(F32),
                                        ALU.subtract).then_inc(lo_ready, 1)

            keep_rest(0)
            make_one_hot(dve, 0, 0)
            for q in range(1, SPLIT_LEAD):
                keep_rest(q)
            for kind, i in FIRST_STEPS:
                drain_e("dve", dve, FIRST, SLOTS - 1, kind, i)
                if (kind, i) in MAKE_AFTER:
                    make_one_hot(dve, 0, MAKE_AFTER[kind, i])
                if kind == "OH" and i + SPLIT_LEAD < NOH:
                    keep_rest(i + SPLIT_LEAD)
            nc.vector.memset(et[:, 1, :, NF:STRIP], 0.0).then_inc(pads_ready, 1)
            make_one_hot(dve, 1, 0)
            dve.wait_ge(b1_ready, 1)
            dve.wait_ge(y_weights_in, 32)
            dve.sem_inc(y_ready, 1)
            with dve.Fori(0, UNITS // SLOTS - 1) as k:
                drain_steps("dve", dve, SLOTS * k, 0, True, True)
                drain_steps("dve", dve, SLOTS * k + 1, 1, True, True)
            drain_steps("dve", dve, UNITS - 2, 0, True, False)
            drain_steps("dve", dve, LAST, 1, False, False)


NAMES = (["dense_ctx", "ids"] + [f"tbl_{f}" for f in range(27)]
         + ["W_top1", "b_top1", "W_top2", "b_top2", "W_top3"])


def kernel(**inputs):
    import numpy as np
    import concourse.bacc as bacc
    from concourse.bass_utils import run_bass_kernel_spmd

    nc = bacc.Bacc("TRN2", target_bir_lowering=False, num_devices=1)
    arrays, aps = {}, {}
    for name in NAMES:
        a = np.ascontiguousarray(inputs[name])
        arrays["in_" + name] = a
        aps[name] = nc.dram_tensor("in_" + name, a.shape, mybir.dt.from_np(a.dtype), kind="ExternalInput").ap()
    out = nc.dram_tensor("out_y", (inputs["ids"].shape[0], 1), F32, kind="ExternalOutput").ap()
    tables = [aps[n] for n in NAMES if n.startswith("tbl_")]
    dlrm_tower(nc, aps["dense_ctx"], aps["ids"], tables, aps["W_top1"], aps["b_top1"], aps["W_top2"],
               aps["b_top2"], aps["W_top3"], out)
    result = run_bass_kernel_spmd(nc, [arrays], core_ids=[0])
    return result.results[0]["out_y"]
```
